# Optimizing a Trainium2 kernel written in Bass

```python
import numpy as np
import jax
import jax.numpy as jnp

def _softmax(x, axis=-1):
    return jax.nn.softmax(x, axis=axis)

def _gelu(x):
    return jax.nn.gelu(x, approximate=True)

def _silu(x):
    return jax.nn.silu(x)

def _sigmoid(x):
    return jax.nn.sigmoid(x)

def _layernorm(x, axis=-1, eps=1e-05):
    m = jnp.mean(x, axis=axis, keepdims=True)
    v = jnp.var(x, axis=axis, keepdims=True)
    return (x - m) / jnp.sqrt(v + eps)

def _scatter_add(tgt, idx, src, axis=0):
    return tgt.at[idx].add(src)

def _segment_sum(src, seg, n):
    return jax.ops.segment_sum(src, seg, n)
kernel_name = 'mk_seq_preln_d1_jaxref_r4_441ce6'

def setup_inputs(seed: int=0):
    np.random.seed(seed)
    _w = jnp.asarray

    def _L0_attn_setup():
        import jax, jax.numpy as jnp
        import numpy as np
        D_MODEL = 256
        NHEAD = 16
        D_K = D_MODEL // NHEAD
        MAX_REL = 256
        key = jax.random.key(seed)
        ks = jax.random.split(key, 6)
        B, S = (4, 512)
        s = 1.0 / np.sqrt(D_MODEL)
        x = jax.random.normal(ks[0], (B, S, D_MODEL), dtype=jnp.float32)
        W_qkv = jax.random.normal(ks[1], (D_MODEL, 3 * D_MODEL), dtype=jnp.float32) * s
        b_qkv = jnp.zeros((3 * D_MODEL,), dtype=jnp.float32)
        W_out = jax.random.normal(ks[2], (D_MODEL, D_MODEL), dtype=jnp.float32) * s
        b_out = jnp.zeros((D_MODEL,), dtype=jnp.float32)
        rel_bias = jax.random.normal(ks[3], (2 * MAX_REL + 1, NHEAD), dtype=jnp.float32) * 0.02
        return {'x': x, 'W_qkv': W_qkv, 'b_qkv': b_qkv, 'W_out': W_out, 'b_out': b_out, 'rel_bias': rel_bias}
    _L0_attn_in = _L0_attn_setup()

    def _L0_ffn_setup():
        import jax, jax.numpy as jnp
        import numpy as np
        B, N, C, H, REG = (1, 2309, 256, 16, 5)
        D = C // H
        key = jax.random.key(seed)
        k0, k1, k2, k3 = jax.random.split(key, 4)
        x = jax.random.normal(k0, (B, N, C), dtype=jnp.float32)
        g_info = jax.random.normal(k1, (12, 2, C), dtype=jnp.float32)
        W_qkv = jax.random.normal(k2, (C, 3 * C), dtype=jnp.float32) * 0.02
        W_proj = jax.random.normal(k3, (C, C), dtype=jnp.float32) * 0.02
        b_proj = jnp.zeros((C,), dtype=jnp.float32)
        return {'x': x, 'g_info': g_info, 'W_qkv': W_qkv, 'W_proj': W_proj, 'b_proj': b_proj}
    _L0_ffn_in = _L0_ffn_setup()
    _d = {'L0_attn_x': _L0_attn_in['x'], 'L0_attn_W_qkv': _L0_attn_in['W_qkv'], 'L0_attn_b_qkv': _L0_attn_in['b_qkv'], 'L0_attn_W_out': _L0_attn_in['W_out'], 'L0_attn_b_out': _L0_attn_in['b_out'], 'L0_attn_rel_bias': _L0_attn_in['rel_bias'], 'L0_ffn_g_info': _L0_ffn_in['g_info'], 'L0_ffn_W_qkv': _L0_ffn_in['W_qkv'], 'L0_ffn_W_proj': _L0_ffn_in['W_proj'], 'L0_ffn_b_proj': _L0_ffn_in['b_proj']}
    _x0 = _d['L0_attn_x']
    _d['L0_attn_x'] = jax.random.normal(jax.random.fold_in(jax.random.key(seed), 1), (4, 1024, 256), dtype=_x0.dtype)
    del _x0
    return _d

def reference(L0_attn_x, L0_attn_W_qkv, L0_attn_b_qkv, L0_attn_W_out, L0_attn_b_out, L0_attn_rel_bias, L0_ffn_g_info, L0_ffn_W_qkv, L0_ffn_W_proj, L0_ffn_b_proj):

    def _L0_attn_ref(x, W_qkv, b_qkv, W_out, b_out, rel_bias):
        import jax, jax.numpy as jnp
        import numpy as np
        D_MODEL = 256
        NHEAD = 16
        D_K = D_MODEL // NHEAD
        MAX_REL = 256
        B, S, D = x.shape
        qkv = x @ W_qkv + b_qkv
        qkv = qkv.reshape(B, S, 3, NHEAD, D_K)
        q, k, v = (qkv[:, :, 0], qkv[:, :, 1], qkv[:, :, 2])
        scores = jnp.einsum('bihd,bjhd->bhij', q, k) / jnp.sqrt(jnp.float32(D_K))
        idxs = jnp.arange(S)
        rel = jnp.clip(idxs[:, None] - idxs[None, :] + MAX_REL, 0, 2 * MAX_REL)
        bias = rel_bias[rel]
        scores = scores + jnp.transpose(bias, (2, 0, 1))[None]
        attn = jax.nn.softmax(scores, axis=-1)
        out = jnp.einsum('bhij,bjhd->bihd', attn, v).reshape(B, S, D)
        return out @ W_out + b_out

    def _L0_ffn_ref(x, g_info, W_qkv, W_proj, b_proj):
        import jax, jax.numpy as jnp
        import numpy as np
        B, N, C, H, REG = (1, 2309, 256, 16, 5)
        D = C // H
        Bx, Nx, Cx = x.shape
        scale = D ** (-0.5)
        qkv = (x @ W_qkv).reshape(Bx, Nx, 3, H, D)
        q, k, v = (qkv[:, :, 0], qkv[:, :, 1], qkv[:, :, 2])
        g_layer = g_info[0].reshape(-1, H, D)
        q_g = g_layer[0]
        q_pure = q[:, REG:]
        q_n = q_pure / jnp.linalg.norm(q_pure, axis=-1, keepdims=True)
        qg_n = q_g / jnp.linalg.norm(q_g, axis=-1, keepdims=True)
        sim = (qg_n[None, None] * q_n).sum(-1).mean(-1)
        sim = (sim - sim.min()) / (sim.max() - sim.min())
        pos = sim > 0.9
        logits = jnp.einsum('bqhd,bkhd->bhqk', q * scale, k)

        def masked_attn(tok_mask):
            key_mask = jnp.concatenate([jnp.ones((Bx, REG), bool), tok_mask], axis=1)
            l = jnp.where(key_mask[:, None, None, :], logits, -jnp.inf)
            a = jax.nn.softmax(l, axis=-1)
            return jnp.einsum('bhqk,bkhd->bqhd', a, v)
        x_pos = masked_attn(pos)
        x_neg = masked_attn(~pos)
        reg_out = (x_pos[:, :REG] + x_neg[:, :REG]) * 0.5
        tok_out = jnp.where(pos[:, :, None, None], x_pos[:, REG:], x_neg[:, REG:])
        out = jnp.concatenate([reg_out, tok_out], axis=1).reshape(Bx, Nx, Cx)
        return out @ W_proj + b_proj
    x = L0_attn_x
    x = x + _L0_attn_ref(_layernorm(x, axis=-1), L0_attn_W_qkv, L0_attn_b_qkv, L0_attn_W_out, L0_attn_b_out, L0_attn_rel_bias)
    x = x + _L0_ffn_ref(_layernorm(x, axis=-1), L0_ffn_g_info, L0_ffn_W_qkv, L0_ffn_W_proj, L0_ffn_b_proj)
    return x

_drawn_inputs = setup_inputs


def setup_inputs(seed=0):
    import zlib

    import numpy as np

    out = dict(_drawn_inputs(seed))
    spreads = {'L0_attn_b_qkv': (0.0, 0.1), 'L0_attn_b_out': (0.0, 0.1), 'L0_ffn_b_proj': (0.0, 0.1)}
    factors = {'L0_attn_rel_bias': 52.86,
     'L0_ffn_g_info': 8.0,
     'L0_ffn_W_qkv': 4.18,
     'L0_ffn_W_proj': 3.565}
    for name, (base, spread) in spreads.items():
        noise = np.random.default_rng([zlib.crc32(name.encode()), seed]).standard_normal(out[name].shape)
        drawn = base * np.exp(spread * noise) if base else spread * noise
        out[name] = jnp.asarray(drawn.astype(out[name].dtype))
    for name, factor in factors.items():
        out[name] = (out[name] * factor).astype(out[name].dtype)
    return out
```

```python
import concourse.bass as bass
from concourse import mybir
from contextlib import ExitStack

F32 = mybir.dt.float32
BF16 = mybir.dt.bfloat16
ALU = mybir.AluOpType
ACT = mybir.ActivationFunctionType
AX = mybir.AxisListType.X

B, S, D = 4, 1024, 256
H, DK = 16, 16
MAX_REL, REG = 256, 5
P = 128
TT = S // P
NT = B * TT
QUADS, HQ = 4, 4
HALF = 512
EPS = 1e-5
BIG = 1e30
THRESHOLD = 0.9

Q_TERMS = (0, 1, 2, 0, 1, 0)
K_TERMS = (2, 1, 0, 1, 0, 0)
RUNS = (3, 2, 1)
TERM_ROWS = len(Q_TERMS) * DK
EXT = 2 * S
LINE0 = S - 1 + MAX_REL
NEAR_LO, NEAR_HI = 5, 9
NEAR0 = NEAR_LO * P
NEAR_W = (NEAR_HI - NEAR_LO + 1) * P
FAR_ROWS = 3 * TT
RB = 2 * MAX_REL + 1
ORDER = "01m2m3mpxm"

ROWS_1 = dict(max=TERM_ROWS, score=TERM_ROWS + 3 + FAR_ROWS, m=TERM_ROWS)
ROWS_2 = dict(max=TERM_ROWS + 2, score=TERM_ROWS + 5, m=TERM_ROWS + 2)


def near_columns(qh, kt):
    lo = max(NEAR_LO - kt, 4 * qh)
    hi = min(NEAR_HI - kt, 4 * qh + 3)
    if lo > hi:
        return None
    return (lo - 4 * qh) * P, (hi - lo + 1) * P, (lo + kt) * P - NEAR0


class Kit:

    def __init__(self, nc, ctx, tag):
        self.nc, self.ctx, self.tag = nc, ctx, tag

    def sb(self, name, shape, dt):
        return self.ctx.enter_context(self.nc.sbuf_tensor(f"{self.tag}_{name}", shape, dt))

    def ps(self, name, shape, dt=F32):
        return self.ctx.enter_context(self.nc.psum_tensor(f"{self.tag}_{name}", shape, dt))

    def sem(self, name):
        return self.nc.alloc_semaphore(f"{self.tag}_{name}")


def constants(nc, keep):
    ident = keep.sb("ident", [P, P], F32)
    identb = keep.sb("identb", [P, P], BF16)
    with ExitStack() as ctx:
        k = Kit(nc, ctx, "c")
        zeroed, done = k.sem("zeroed"), k.sem("done")
        block = ctx.enter_context(nc.Block())

        @block.gpsimd
        def _(pool):
            pool.memset(ident[:, :], 0.0).then_inc(zeroed, 1)
            pool.memset(identb[:, :], 0.0).then_inc(zeroed, 1)
            pool.wait_ge(zeroed, 2)
            for m in (ident, identb):
                pool.affine_select(out=m[:, :], in_=m[:, :], compare_op=ALU.not_equal, fill=1.0, base=0,
                                   pattern=[[-1, P]], channel_multiplier=1).then_inc(done, 1)
            pool.wait_ge(done, 2)
    return ident, identb


def bias_lines(nc, ident, rel_bias, line_dram, near_dram, far_dram):
    with ExitStack() as ctx:
        k = Kit(nc, ctx, "bl")
        rb = k.sb("rb", [P, 5, H], F32)
        bT = k.sb("bT", [H, RB], F32)
        line = k.sb("line", [H, EXT], F32)
        rest = k.sb("rest", [H, NEAR_W + P], F32)
        near = k.sb("near", [H, 3, NEAR_W + P], BF16)
        far = k.sb("far", [H, 3, TT, S], BF16)
        bank = k.ps("bank", [H, 2 * HALF])
        loaded, turned, step, far0, fars, stored = (
            k.sem(n) for n in ("loaded", "turned", "step", "far0", "fars", "stored"))
        block = ctx.enter_context(nc.Block())
        full = RB // P
        hi_end = LINE0 - 2 * MAX_REL
        lo_at = LINE0

        @block.sync
        def _(sp):
            sp.dma_start(rb[:, 0:full, :], rel_bias[0:full * P, :].rearrange("(t p) h -> p t h", p=P)).then_inc(loaded, 16)
            sp.dma_start(rb[0:1, full, :], rel_bias[full * P:RB, :]).then_inc(loaded, 16)
            sp.wait_ge(step, 2)
            sp.dma_start(line_dram, line[:, :]).then_inc(stored, 16)
            sp.wait_ge(step, 6)
            sp.dma_start(near_dram, near[:, :, :]).then_inc(stored, 16)
            sp.wait_ge(fars, 5 + 5)
            sp.dma_start(far_dram, far[:, :, :, :].rearrange("h a t n -> h (a t) n")).then_inc(stored, 16)
            sp.wait_ge(stored, 48)

        @block.tensor
        def _(pe):
            pe.wait_ge(loaded, 32)
            for t in range(full):
                nc.tensor.transpose(bank[0:H, t * P:(t + 1) * P], rb[:, t, :], ident[:, :])
            nc.tensor.transpose(bank[0:H, full * P:RB], rb[0:1, full, :], ident[0:1, 0:1]).then_inc(turned, 1)

        @block.gpsimd
        def _(pool):
            pool.memset(far[:, 1:3, :, :], 0.0).then_inc(far0, 1)

        @block.vector
        def _(dve):
            n = [0]

            def chained(ins):
                n[0] += 1
                ins.then_inc(step, 1)
                dve.wait_ge(step, n[0])

            dve.memset(far[:, 0, :, :], 0.0).then_inc(far0, 1)
            dve.wait_ge(turned, 1)
            chained(dve.tensor_copy(bT[:, :], bank[0:H, 0:RB]))
            dve.tensor_copy(line[:, 0:hi_end], bT[:, RB - 1:RB].to_broadcast([H, hi_end]))
            dve.tensor_copy(line[:, lo_at + 1:EXT], bT[:, 0:1].to_broadcast([H, EXT - lo_at - 1]))
            chained(dve.tensor_copy(line[:, hi_end:lo_at + 1], bT[:, ::-1]))
            src = line[:, NEAR0:NEAR0 + NEAR_W + P]
            chained(dve.tensor_copy(near[:, 0, :], src))
            chained(dve.tensor_tensor(rest[:, :], src, near[:, 0, :], ALU.subtract))
            chained(dve.tensor_copy(near[:, 1, :], rest[:, :]))
            chained(dve.tensor_tensor(near[:, 2, :], rest[:, :], near[:, 1, :], ALU.subtract))
            dve.wait_ge(far0, 2)
            for kt in range(TT):
                below, above = NEAR_LO - kt, NEAR_HI + 1 - kt
                if below > 0:
                    dve.tensor_copy(far[:, :, kt, 0:below * P], near[:, :, 0:1].to_broadcast([H, 3, below * P])).then_inc(fars, 1)
                if above < TT:
                    dve.tensor_copy(far[:, :, kt, above * P:S],
                                    near[:, :, NEAR_W + P - 1:NEAR_W + P].to_broadcast([H, 3, S - above * P])).then_inc(fars, 1)


def prepare(nc, layer, ident, x_in, w_qkv, b_qkv, g_info, v_sb, parts_dram, mask_dram):
    second = layer == 2
    FT = 2 * D // P
    with ExitStack() as ctx:
        k = Kit(nc, ctx, f"p{layer}")
        w = k.sb("w", [P, 2, 3 * D], F32)
        x = k.sb("x", [P, TT, D], F32)
        xn = k.sb("xn", [P, TT, D], F32)
        xT = k.sb("xT", [P, 2, S], F32)
        bst = k.sb("bst", [P, TT, 6], F32)
        mv = k.sb("mv", [P, TT, 2], F32)
        ve, sd, rs, r2, vr, nw, rstd = (k.sb(n, [P, TT], F32) for n in ("ve", "sd", "rs", "r2", "vr", "nw", "rstd"))
        full = k.sb("full", [P, 2, S], F32)
        rest = k.sb("rest", [P, 2, S], F32)
        part = k.sb("part", [P, 3, FT, S], BF16)
        banks = k.ps("banks", [P, 8, HALF])
        proj = [banks[:, 0:2, :], banks[:, 2:4, :]]
        turn_bank = [banks[:, 4, :], banks[:, 5, :]]
        nat = [banks[:, 6, :], banks[:, 7, :]]
        if second:
            qn = k.sb("qn", [P, TT, D], F32)
            qsq = k.sb("qsq", [P, TT, D], F32)
            qg = k.sb("qg", [P, TT, D], F32)
            num = k.sb("num", [P, NT, H], F32)
            sq = k.sb("sq", [P, NT, H], F32)
            gq, gsq, gn = (k.sb(n, [P, D], F32) for n in ("gq", "gsq", "gn"))
            gss, gnorm, grec = (k.sb(n, [P, H], F32) for n in ("gss", "gnorm", "grec"))
        else:
            bq = k.sb("bq", [P, FT], F32)
            bqs = k.sb("bqs", [P, FT], F32)
            bv = k.sb("bv", [P, D], F32)
        (w_in, x_here, g_in, stats, gate, var_done, sqrt_done, step, xn_done, turned, xT_done, proj_done, full_done,
         part0, part1, part2, rest_done, part_out, nat_done, v_done) = (k.sem(n) for n in (
             "w_in", "x_here", "g_in", "stats", "gate", "var_done", "sqrt_done", "step", "xn_done", "turned", "xT_done",
             "proj_done", "full_done", "part0", "part1", "part2", "rest_done", "part_out", "nat_done", "v_done"))
        if second:
            qn_done, squares, prods, sums, g_sum, g_root = (
                k.sem(n) for n in ("qn_done", "squares", "prods", "sums", "g_sum", "g_root"))
        else:
            bias_done = k.sem("bias_done")
        over = ExitStack()
        block = over.enter_context(nc.Block())
        x_v = x_in.rearrange("(b t p) d -> b p t d", p=P, t=TT)
        OUTS = 3 * FT * 16

        @block.sync
        def _(sp):
            sp.sem_inc(part_out, 16)
            sp.dma_start(x[:, :, :], x_v[0]).then_inc(x_here, 16)
            sp.dma_start(w[:, :, :], w_qkv.rearrange("(c p) n -> p c n", p=P)).then_inc(w_in, 16)
            if second:
                sp.dma_start(gq[:, :], g_info[0, 0:1, :].to_broadcast([P, D])).then_inc(g_in, 16)
            else:
                sp.dma_start(bv[:, :], b_qkv[2 * D:3 * D].rearrange("(a n) -> a n", a=1).to_broadcast([P, D])).then_inc(g_in, 16)
                with nc.allow_non_contiguous_dma(reason="512 biases"):
                    sp.dma_start(bq[:, :], b_qkv[0:2 * D].rearrange("(f p) -> p f", p=P)).then_inc(g_in, 16)

            def load_x(b):
                sp.wait_ge(xn_done, b)
                sp.dma_start(x[:, :, :], x_v[bass.ds(b, 1), :, :, :].rearrange("a p t d -> (a p) t d")).then_inc(x_here, 16)

            def batch(b, more):
                for f in range(FT):
                    for i, done in enumerate((part0, part1, part2)):
                        sp.wait_ge(done, b * FT + f + 1)
                        heads = slice((f % 2) * (P // DK), (f % 2 + 1) * (P // DK))
                        dst = parts_dram[f // 2, heads, place_of_part(f // 2, i), :, :]
                        sp.dma_start(dst[:, :, bass.ds(b * S, S)], part[:, i, f, :]).then_inc(part_out, 16)
                    if f == 1 and more:
                        load_x(b + 2)

            load_x(1)
            with sp.Fori(0, B - 2) as b:
                batch(b, True)
            batch(B - 2, False)
            batch(B - 1, False)
            sp.wait_ge(part_out, B * OUTS + 16)

        @block.tensor
        def _(pe):
            pe.sem_inc(nat_done, 1)
            pe.wait_ge(w_in, 16)
            def turns(b, chosen):
                pe.wait_ge(xn_done, b + 1)
                for i in chosen:
                    c, t4 = i // 2, i % 2
                    pe.wait_ge(xT_done, b * 4 + max(i, 1))
                    for t in range(4):
                        last = nc.tensor.transpose(turn_bank[i % 2][:, t * P:(t + 1) * P],
                                                   xn[:, 4 * t4 + t, c * P:(c + 1) * P], ident[:, :])
                    last.then_inc(turned, 1)

            def batch(b, more):
                turns(b, (2, 3))
                pe.wait_ge(xT_done, b * 4 + 4 + 1)
                for f in range(FT):
                    if f == FT - 1 and more:
                        turns(b + 1, (0, 1))
                    pe.wait_ge(full_done, b * FT + max(f, 1))
                    for hf in range(2):
                        for c in range(2):
                            last = nc.tensor.matmul(proj[f % 2][:, hf, :], w[:, c, f * P:(f + 1) * P],
                                                    xT[:, c, hf * HALF:(hf + 1) * HALF], start=c == 0, stop=c == 1)
                    last.then_inc(proj_done, 1)
                    for t in (2 * f, 2 * f + 1):
                        pe.wait_ge(v_done, b * TT + max(t, 1))
                        for c in range(2):
                            w3 = w[:, c, :].rearrange("p (a n) -> p a n", n=D)
                            last = nc.tensor.matmul(nat[t % 2] if second else nat[t % 2][:, 0:D],
                                                    xT[:, c, t * P:(t + 1) * P],
                                                    w3[:, 0:3:2, :] if second else w3[:, 2, :], start=c == 0, stop=c == 1)
                        last.then_inc(nat_done, 1)

            turns(0, (0, 1))
            with pe.Fori(0, B - 1) as b:
                batch(b, True)
            batch(B - 1, False)

        @block.scalar
        def _(act):
            act.sem_inc(full_done, 1)
            if second:
                act.wait_ge(g_sum, 1)
                act.activation(gnorm[:, :], gss[:, :], ACT.Sqrt).then_inc(g_root, 1)
            else:
                act.wait_ge(bias_done, 1)
            def root(b):
                act.wait_ge(var_done, b + 1)
                act.activation(sd[:, :], ve[:, :], ACT.Sqrt).then_inc(sqrt_done, 1)

            def batch(b, more):
                for f in range(FT):
                    act.wait_ge(proj_done, b * FT + f + 1)
                    act.wait_ge(rest_done, b * FT + max(f, 1))
                    dst = full[:, f % 2, :]
                    if not second and f < 2:
                        dst = full[:, f % 2, ::-1]
                    src = proj[f % 2].rearrange("p a n -> p (a n)")
                    scale = DK ** -0.5 if f < 2 else 1.0
                    if second:
                        act.activation(dst, src, ACT.Copy, scale=scale).then_inc(full_done, 1)
                    else:
                        act.activation(dst, src, ACT.Identity, scale=scale, bias=bqs[:, f:f + 1]).then_inc(full_done, 1)
                    if f == 1 and more:
                        root(b + 1)
                if second:
                    act.wait_ge(qn_done, (b + 1) * TT)
                    act.wait_ge(sums, b * 2 + 1)
                    act.activation(qsq[:, :, :], qn[:, :, :], ACT.Square).then_inc(squares, 1)

            root(0)
            with act.Fori(0, B - 1) as b:
                batch(b, True)
            batch(B - 1, False)

        @block.gpsimd
        def _(pool):
            pool.sem_inc(rest_done, 1)
            with pool.Fori(0, B) as b:
                for f in range(FT):
                    pool.wait_ge(part0, b * FT + f + 1)
                    pool.tensor_tensor(rest[:, f % 2, :], full[:, f % 2, :], part[:, 0, f, :], ALU.subtract).then_inc(rest_done, 1)
                    pool.wait_ge(part1, b * FT + f + 1)
                    pool.wait_ge(rest_done, b * FT + f + 1 + 1)
                    pool.wait_ge(part_out, b * OUTS + 16)
                    pool.tensor_tensor(part[:, 2, f, :], rest[:, f % 2, :], part[:, 1, f, :], ALU.subtract).then_inc(part2, 1)
                if second:
                    pool.wait_ge(qn_done, (b + 1) * TT)
                    pool.wait_ge(sums, b * 2 + 1)
                    pool.tensor_tensor(qg[:, :, :], qn[:, :, :], gn[:, :].unsqueeze(1).to_broadcast([P, TT, D]),
                                       ALU.mult).then_inc(prods, 1)

        @block.vector
        def _(dve):
            dve.sem_inc(xT_done, 1)
            dve.sem_inc(v_done, 1)
            off = 0
            if second:
                dve.sem_inc(sums, 1)
                heads = lambda t: t[:, :].rearrange("p (h d) -> p h d", d=DK)
                dve.wait_ge(g_in, 16)
                dve.tensor_tensor(gsq[:, :], gq[:, :], gq[:, :], ALU.mult).then_inc(step, 1)
                dve.wait_ge(step, 1)
                dve.tensor_reduce(gss[:, :], heads(gsq), AX, ALU.add).then_inc(g_sum, 1)
                dve.wait_ge(g_root, 1)
                dve.reciprocal(grec[:, :], gnorm[:, :]).then_inc(step, 1)
                dve.wait_ge(step, 2)
                dve.tensor_tensor(heads(gn), heads(gq), grec[:, :].unsqueeze(2).to_broadcast([P, H, DK]),
                                  ALU.mult).then_inc(step, 1)
                dve.wait_ge(step, 3)
                off = 3
            else:
                dve.wait_ge(g_in, 32)
                dve.tensor_scalar(bqs[:, 0:2], bq[:, 0:2], DK ** -0.5, None, ALU.mult)
                dve.tensor_copy(bqs[:, 2:4], bq[:, 2:4]).then_inc(bias_done, 1)
            def variance(b):
                dve.wait_ge(x_here, b * 16 + 16)
                for t in range(TT):
                    dve.bn_stats(bst[:, t, :], x[:, t, :]).then_inc(stats, 1)
                dve.wait_ge(stats, b * 2 * TT + TT)
                dve.sem_inc(gate, 1)
                for t in range(TT):
                    dve.bn_aggr(mv[:, t, :], bst[:, t, :]).then_inc(stats, 1)
                dve.wait_ge(stats, b * 2 * TT + 2 * TT)
                dve.tensor_scalar(ve[:, :], mv[:, :, 1], EPS, None, ALU.add).then_inc(var_done, 1)

            def scale(b):
                dve.wait_ge(sqrt_done, b + 1)
                dve.reciprocal(rs[:, :], sd[:, :]).then_inc(step, 1)
                dve.wait_ge(step, b * 5 + off + 1)
                dve.tensor_tensor(r2[:, :], rs[:, :], rs[:, :], ALU.mult).then_inc(step, 1)
                dve.wait_ge(step, b * 5 + off + 2)
                dve.tensor_tensor(vr[:, :], r2[:, :], ve[:, :], ALU.mult).then_inc(step, 1)
                dve.wait_ge(step, b * 5 + off + 3)
                dve.tensor_scalar(nw[:, :], vr[:, :], -0.5, 1.5, ALU.mult, ALU.add).then_inc(step, 1)
                dve.wait_ge(step, b * 5 + off + 4)
                dve.tensor_tensor(rstd[:, :], rs[:, :], nw[:, :], ALU.mult).then_inc(step, 1)
                dve.wait_ge(step, b * 5 + off + 5)
                for t in range(TT):
                    last = dve.tensor_scalar(xn[:, t, :], x[:, t, :], mv[:, t, 0:1], rstd[:, t:t + 1], ALU.subtract, ALU.mult)
                last.then_inc(xn_done, 1)

            def turned_out(b):
                for i in range(4):
                    c, t4 = i // 2, i % 2
                    dve.wait_ge(turned, b * 4 + i + 1)
                    dve.wait_ge(nat_done, b * TT + 1)
                    dve.tensor_copy(xT[:, c, t4 * HALF:(t4 + 1) * HALF], turn_bank[i % 2]).then_inc(xT_done, 1)

            def batch(b, more):
                def first_part(f):
                    dve.wait_ge(full_done, b * FT + f + 1 + 1)
                    dve.wait_ge(part_out, b * OUTS + 16)
                    dve.tensor_copy(part[:, 0, f, :], full[:, f % 2, :]).then_inc(part0, 1)

                def second_part(f):
                    dve.wait_ge(rest_done, b * FT + f + 1 + 1)
                    dve.tensor_copy(part[:, 1, f, :], rest[:, f % 2, :]).then_inc(part1, 1)

                for f in range(FT):
                    first_part(f)
                    for t in (2 * f, 2 * f + 1):
                        dve.wait_ge(nat_done, b * TT + t + 1 + 1)
                        dst = v_sb[:, bass.ds(b * TT + t, 1), :, :].rearrange("p a h d -> p (a h d)")
                        if second:
                            dve.tensor_copy(qn[:, t, :], nat[t % 2][:, 0:D]).then_inc(qn_done, 1)
                            dve.tensor_copy(dst, nat[t % 2][:, D:2 * D]).then_inc(v_done, 1)
                        else:
                            dve.tensor_tensor(dst, nat[t % 2][:, 0:D], bv[:, :], ALU.add).then_inc(v_done, 1)
                    if f == 0 and more:
                        variance(b + 1)
                    if f == 1 and more:
                        scale(b + 1)
                    if f == FT - 1 and more:
                        turned_out(b + 1)
                    second_part(f)
                if second:
                    out = lambda t: t[:, bass.ds(b * TT, TT), :].rearrange("p t h -> p (t h)")
                    dve.wait_ge(squares, b + 1)
                    dve.tensor_reduce(out(sq), qsq[:, :, :].rearrange("p t (h d) -> p (t h) d", d=DK), AX, ALU.add).then_inc(sums, 1)
                    dve.wait_ge(prods, b + 1)
                    dve.tensor_reduce(out(num), qg[:, :, :].rearrange("p t (h d) -> p (t h) d", d=DK), AX, ALU.add).then_inc(sums, 1)

            variance(0)
            scale(0)
            turned_out(0)
            with dve.Fori(0, B - 1) as b:
                batch(b, True)
            batch(B - 1, False)

        over.close()
        if second:
            similarity_masks(nc, ident, banks[:, 0, :], num, sq, mask_dram)


def similarity_masks(nc, ident, bank, num, sq, mask_dram):
    with ExitStack() as ctx:
        k = Kit(nc, ctx, "sm")
        flat = lambda t: t[:, :, :].rearrange("p t h -> p (t h)")
        root, rec, r2, nw, prod = (k.sb(n, [P, NT, H], F32) for n in ("root", "rec", "r2", "nw", "prod"))
        sim, place, pos = (k.sb(n, [P, NT], F32) for n in ("sim", "place", "pos"))
        ends, ends_all = k.sb("ends", [P, 2], F32), k.sb("ends_all", [P, 2], F32)
        span = k.sb("span", [P, 2], F32)
        kinds = k.sb("kinds", [P, 4, NT], F32)
        rows = k.sb("rows", [P, P], BF16)
        roots, step, ends_done, all_done, kinds_done, turned, rows_done, stored = (
            k.sem(n) for n in ("roots", "step", "ends_done", "all_done", "kinds_done", "turned", "rows_done", "stored"))
        block = ctx.enter_context(nc.Block())

        @block.scalar
        def _(act):
            act.activation(flat(root), flat(sq), ACT.Sqrt).then_inc(roots, 1)

        @block.gpsimd
        def _(pool):
            pool.wait_ge(ends_done, 2)
            pool.partition_all_reduce(ends_all[:, :], ends[:, :], P, bass.bass_isa.ReduceOp.max).then_inc(all_done, 1)

        @block.tensor
        def _(pe):
            pe.wait_ge(kinds_done, 1)
            nc.tensor.transpose(bank[:, 0:P], kinds[:, :, :].rearrange("p k t -> p (k t)"), ident[:, :]).then_inc(turned, 1)

        @block.sync
        def _(sp):
            sp.wait_ge(rows_done, 1)
            sp.dma_start(mask_dram.rearrange("k (t n) -> (k t) n", n=P), rows[:, :]).then_inc(stored, 16)
            sp.wait_ge(stored, 16)

        @block.vector
        def _(dve):
            count = [0]

            def chained(ins):
                count[0] += 1
                ins.then_inc(step, 1)
                dve.wait_ge(step, count[0])

            dve.wait_ge(roots, 1)
            chained(dve.reciprocal(flat(rec), flat(root)))
            chained(dve.tensor_tensor(flat(r2), flat(rec), flat(rec), ALU.mult))
            chained(dve.tensor_tensor(flat(prod), flat(r2), flat(sq), ALU.mult))
            chained(dve.tensor_scalar(flat(nw), flat(prod), -0.5, 1.5, ALU.mult, ALU.add))
            chained(dve.tensor_tensor(flat(r2), flat(rec), flat(nw), ALU.mult))
            chained(dve.tensor_tensor(flat(prod), flat(num), flat(r2), ALU.mult))
            chained(dve.tensor_reduce(place[:, :], prod[:, :, :], AX, ALU.add))
            chained(dve.tensor_scalar(sim[:, :], place[:, :], 1.0 / H, None, ALU.mult))
            chained(dve.tensor_copy(sim[0:REG, 0:NT:TT], sim[0:REG, 1:NT:TT]))
            dve.tensor_reduce(ends[:, 0:1], sim[:, :], AX, ALU.max).then_inc(ends_done, 1)
            dve.tensor_reduce(ends[:, 1:2], sim[:, :], AX, ALU.min, negate=True).then_inc(ends_done, 1)
            dve.wait_ge(all_done, 1)
            chained(dve.tensor_tensor(span[:, 0:1], ends_all[:, 0:1], ends_all[:, 1:2], ALU.add))
            chained(dve.reciprocal(span[:, 1:2], span[:, 0:1]))
            chained(dve.tensor_scalar(place[:, :], sim[:, :], ends_all[:, 1:2], span[:, 1:2], ALU.add, ALU.mult))
            chained(dve.tensor_scalar(pos[:, :], place[:, :], THRESHOLD, None, ALU.is_gt))
            dve.tensor_scalar(kinds[:, 0, :], pos[:, :], 1.0, BIG, ALU.subtract, ALU.mult)
            dve.tensor_scalar(kinds[:, 1, :], pos[:, :], -BIG, None, ALU.mult)
            dve.tensor_copy(kinds[:, 2, :], pos[:, :])
            chained(dve.tensor_scalar(kinds[:, 3, :], pos[:, :], -1.0, 1.0, ALU.mult, ALU.add))
            dve.memset(kinds[0:REG, 0, 0:NT:TT], 0.0)
            dve.memset(kinds[0:REG, 1, 0:NT:TT], -BIG)
            dve.memset(kinds[0:REG, 2, 0:NT:TT], 0.0)
            dve.memset(kinds[0:REG, 3, 0:NT:TT], 0.0).then_inc(kinds_done, 1)
            dve.wait_ge(turned, 1)
            dve.tensor_copy(rows[:, :], bank[:, 0:P]).then_inc(rows_done, 1)


def place_of_part(which, part):
    return 2 - part if which else part


def load_terms(sp, which, parts_dram, dst, g, b, columns, loaded):
    n = 0
    for run in RUNS:
        low = place_of_part(which, (Q_TERMS, K_TERMS)[which][n])
        rows = parts_dram[which][bass.ds(g * HQ, HQ), low:low + run, :, b * S:b * S + columns]
        sp.dma_start(dst[n * DK:(n + run) * DK], rows.rearrange("h a d n -> (a d) h n")).then_inc(loaded, 16)
        n += run


def attend(nc, layer, ident, identb, v_sb, parts_dram, mask_dram, line_dram, near_dram, far_dram):
    first = layer == 1
    R = ROWS_1 if first else ROWS_2
    STEPS = 2 * TT
    MAXES = HQ * TT * 2
    PER_STEP = MAXES // STEPS
    AHEAD = 3 * PER_STEP
    SLOTS = B
    TURN_BANKS = 3
    ADD_AFTER = 0
    n_loads = 2 * len(RUNS) + (1 if first else 2)
    with ExitStack() as ctx:
        k = Kit(nc, ctx, f"a{layer}")
        q_sb = k.sb("q", [P, SLOTS, HQ, S], BF16)
        k_sb = k.sb("k", [P, SLOTS, HQ, S], BF16)
        vu = k.sb("vu", [P, 2, TT, HQ, 32], F32)
        RING = 2
        probs = k.sb("probs", [P, RING, HQ, HALF], F32)
        mh = k.sb("mh", [P, HQ, TT, 2], F32)
        mq = k.sb("mq", [P, HQ, TT], F32)
        m1 = k.sb("m1", [HQ * TT, P], F32)
        m2 = k.sb("m2", [HQ * TT, P], F32)
        mparts = k.sb("mparts", [HQ * TT, 3, P], BF16)
        osb = k.sb("osb", [P, HALF], F32)
        rz = k.sb("rz", [P, 4, HQ], F32)
        ones = k.sb("ones", [3, HQ, S], BF16)
        scores = k.ps("scores", [P, 2, 2, HALF])
        outb = k.ps("outb", [P, HALF])
        turnb = k.ps("turnb", [P, TURN_BANKS, HALF])
        if first:
            strip = k.sb("strip", [P, HQ, EXT - P], F32)
            near = k.sb("near", [P, 2, 3, NEAR_W], BF16)
            near_f = k.sb("near_f", [P, 2, NEAR_W], F32)
            hot = k.sb("hot", [TT, HQ, S], BF16)
            summed = k.sb("summed", [P, 4, HALF], BF16)
        loaded = [k.sem(f"loaded{i}") for i in range(SLOTS)]
        if first:
            strip_in = [k.sem(f"strip_in{h}") for h in range(HQ)]
            near_in, gate, added = k.sem("near_in"), k.sem("gate"), k.sem("added")
        (fixed, consts, fills, v_ready, m_rows, score_ready, exp_done,
         pv_done, out_taken, turn_ready, turn_taken, mq_done, mstep, mparts_done, rz_done) = (k.sem(n) for n in (
             "fixed", "consts", "fills", "v_ready", "m_rows",
             "score_ready", "exp_done", "pv_done", "out_taken", "turn_ready", "turn_taken", "mq_done", "mstep",
             "mparts_done", "rz_done"))
        block = ctx.enter_context(nc.Block())
        n_fixed = SLOTS * (4 if first else 1)

        def unit_turns(b, last):
            steps = []
            for j in range(STEPS):
                n = AHEAD + PER_STEP * j
                turns = [("max", 1 + n // MAXES, (n + i) % MAXES) for i in range(PER_STEP)]
                turns = [turn for turn in turns if not (last and b + turn[1] >= B)]
                if j == 1 and b > 0:
                    turns.insert(3, ("out", 1, 1))
                if j == TT + 2:
                    turns.insert(3, ("out", 0, 0))
                if j == STEPS - AHEAD // PER_STEP and not (last and b == B - 1):
                    turns.insert(3, ("rows",))
                steps.append(turns)
            steps.append([("out", 0, 1)] if b == B - 1 else [])
            return steps

        def count(b, last):
            return sum(len(turns) for turns in unit_turns(b, last))

        def place_of(turn, b, last):
            return [t for turns in unit_turns(b, last) for t in turns].index(turn)

        PROLOGUE = MAXES + 1 + AHEAD
        QUAD_TURNS = sum(count(b, False) for b in range(B))

        SHIFT = (count(B - 1, False) - PROLOGUE) % TURN_BANKS

        def base(g, b, last):
            return PROLOGUE + QUAD_TURNS * g + sum(count(i, last) for i in range(b))

        def bank_free(g, b, last, t):
            if t >= TURN_BANKS:
                return base(g, b, last) + t - TURN_BANKS + 1
            before = count((b - 1) % B, last and b > 0)
            return base(g, b, last) - (before - 1 - t) % TURN_BANKS

        def split_max(i):
            return i // (2 * TT), i % (2 * TT) // 2, i % 2

        NEAR_STEPS = [j for j in range(STEPS) if near_columns(j // TT, j % TT)] if first else []

        @block.sync
        def _(sp):
            def load(g, b):
                load_terms(sp, 0, parts_dram, q_sb[:, b], g, b, S, loaded[b])
                load_terms(sp, 1, parts_dram, k_sb[:, b], g, b, S, loaded[b])
                if first:
                    row = R["m"] + 3
                    sp.dma_start(q_sb[row:row + FAR_ROWS, b, :, :],
                                 far_dram[bass.ds(g * HQ, HQ), :, :].rearrange("h r n -> r h n")).then_inc(loaded[b], 16)
                else:
                    for kind, dst in ((0, q_sb), (2, k_sb)):
                        rows = mask_dram[kind:kind + 2, b * S:(b + 1) * S].unsqueeze(1).to_broadcast([2, HQ, S])
                        sp.dma_start(dst[TERM_ROWS:TERM_ROWS + 2, b, :, :], rows).then_inc(loaded[b], 16)

            def store_max(g, b):
                for part in range(3):
                    row = R["m"] + part
                    sp.dma_start(q_sb[row:row + 1, b, :, :].rearrange("o h (t n) -> o (h t) n", n=P),
                                 mparts[:, part, :]).then_inc(m_rows, 16)

            load(0, 0)
            load(0, 1)
            sp.wait_ge(consts, 2 if first else 1)
            for s in range(SLOTS):
                sp.dma_start(k_sb[R["m"]:R["m"] + 3, s, :, :], ones[0:3]).then_inc(fixed, 16)
                for part in range(3 if first else 0):
                    row = R["m"] + 3 + part * TT
                    sp.dma_start(k_sb[row:row + TT, s, :, :], hot[:, :, :]).then_inc(fixed, 16)
            sp.wait_ge(fixed, 16 * n_fixed)

            load(0, 2)
            sp.wait_ge(mparts_done, 1)
            store_max(0, 0)

            def unit(g, b, last):
                if b == 0 or not last:
                    sp.wait_ge(pv_done, (g * B + b) * STEPS + RING)
                    load(g + (b + 3) // B, (b + 3) % B)
                if not (last and b == B - 1):
                    sp.wait_ge(mparts_done, g * B + b + 2)
                    store_max(g + (b + 1) // B, (b + 1) % B)

            with sp.Fori(0, QUADS - 1) as g:
                for b in range(B):
                    unit(g, b, False)
            for b in range(B):
                unit(QUADS - 1, b, True)

        @block.gpsimd
        def _(pool):
            def strip_load(g, h):
                row = line_dram[bass.ds(g * HQ + h, 1), :]
                src = bass.AP(tensor=row.tensor, offset=row.offset, ap=[[1, P], [1, EXT - P]])
                pool.dma_start(strip[:, h, :], src).then_inc(strip_in[h], 16)

            def near_load(g):
                for h in range(2):
                    row = near_dram[bass.ds(g * HQ + h, 1), :, :]
                    src = bass.AP(tensor=row.tensor, offset=row.offset, ap=[[1, P], [NEAR_W + P, 3], [1, NEAR_W]])
                    pool.dma_start(near[:, h, :, :], src).then_inc(near_in, 16)
                for h in range(2):
                    row = line_dram[bass.ds(g * HQ + 2 + h, 1), NEAR0:EXT]
                    src = bass.AP(tensor=row.tensor, offset=row.offset, ap=[[1, P], [1, NEAR_W]])
                    pool.dma_start(near_f[:, h, :], src).then_inc(near_in, 16)

            if first:
                for h in range(HQ):
                    strip_load(0, h)
                near_load(0)
            pool.memset(ones[:, :, :], 1.0).then_inc(consts, 1)
            pool.memset(vu[:, :, :, :, DK:32], 0.0).then_inc(fills, 1)
            pool.wait_ge(fills, 1)
            pool.memset(vu[:, :, :, :, DK:DK + 1], 1.0).then_inc(fills, 1)
            if first:
                pool.memset(hot[:, :, :], 1.0).then_inc(fills, 1)
                pool.wait_ge(fills, 3)
                pool.affine_select(out=hot[:, :, :], in_=hot[:, :, :], compare_op=ALU.is_ge, fill=0.0, base=0,
                                   pattern=[[0, HQ], [1, S]], channel_multiplier=-P).then_inc(fills, 1)
                pool.wait_ge(fills, 4)
                pool.affine_select(out=hot[:, :, :], in_=hot[:, :, :], compare_op=ALU.is_ge, fill=0.0, base=P - 1,
                                   pattern=[[0, HQ], [-1, S]], channel_multiplier=P).then_inc(consts, 1)

            def v_unit(g, b):
                src = v_sb[:, b * TT:(b + 1) * TT, bass.ds(g * HQ, HQ), :]
                pool.tensor_copy(vu[:, b % 2, :, :, 0:DK], src).then_inc(v_ready, 1)

            v_unit(0, 0)

            def unit(g, b, last):
                u = g * B + b
                if not (last and b == B - 1):
                    pool.wait_ge(pv_done, u * STEPS + RING)
                    v_unit(g + (b + 1) // B, (b + 1) % B)
                if first and not last and b == 2:
                    for h in range(HQ):
                        turn = place_of(("max", 1, 2 * TT * (h + 1) - 1), b, last)
                        pool.wait_ge(turn_taken, base(g, b, last) + turn + 1)
                        strip_load(g + 1, h)
                if first and not last and b == 3:
                    pool.wait_ge(pv_done, u * STEPS + NEAR_STEPS[-1] + 1 + RING)
                    near_load(g + 1)

            with pool.Fori(0, QUADS - 1) as g:
                for b in range(B):
                    unit(g, b, False)
            for b in range(B):
                unit(QUADS - 1, b, True)

        @block.tensor
        def _(pe):
            def take_max(g, b, i, bank):
                h, t, hf = split_max(i)
                if i == 0:
                    pe.wait_ge(loaded[b], (g + 1) * 16 * n_loads)
                rows = R["max"]
                nc.tensor.matmul(turnb[:, bank, :], q_sb[0:rows, b, h, t * P:(t + 1) * P],
                                 k_sb[0:rows, b, h, hf * HALF:(hf + 1) * HALF], start=True, stop=True).then_inc(turn_ready, 1)

            def turn_max(u, bank):
                pe.wait_ge(mq_done, u + 1)
                nc.tensor.transpose(turnb[0:HQ * TT, bank, 0:P], mq[:, :, :].rearrange("p h t -> p (h t)"),
                                    ident[:, :]).then_inc(turn_ready, 1)

            def turn_out(u, qh, bank):
                pe.wait_ge(out_taken, u * 2 + qh + 2)
                for t in range(4):
                    last = nc.tensor.transpose(turnb[:, bank, t * P:(t + 1) * P], osb[:, t * P:(t + 1) * P], ident[:, :])
                last.then_inc(turn_ready, 1)

            def score(u, g, b, j, h):
                qh, kt, hp = j // TT, j % TT, h // 2
                if j == 0 and h == 0:
                    pe.wait_ge(m_rows, (u + 1) * 48)
                if first and b == 0 and j == NEAR_STEPS[0] and h == 0:
                    pe.wait_ge(near_in, (g + 1) * HQ * 16)
                rows = R["score"]
                if h % 2 == 0:
                    pe.wait_ge(exp_done, u * 2 * STEPS + 2 * j + hp + 1)
                place = near_columns(qh, kt) if first and hp == 0 else None
                bank = scores[:, hp, h % 2, :]
                last = nc.tensor.matmul(bank, k_sb[0:rows, b, h, kt * P:(kt + 1) * P],
                                        q_sb[0:rows, b, h, qh * HALF:(qh + 1) * HALF], start=True, stop=place is None)
                if place is not None:
                    col, width, at = place
                    for part in range(3):
                        last = nc.tensor.matmul(bank[:, col:col + width], identb[:, :], near[:, h, part, at:at + width],
                                                start=False, stop=part == 2)
                if h % 2:
                    last.then_inc(score_ready, 1)

            def products(u, b, j):
                qh, kt = j // TT, j % TT
                if j == 0:
                    pe.wait_ge(v_ready, u + 1)
                pe.wait_ge(exp_done, u * 2 * STEPS + 2 * j + 2 + 2)
                if kt == 0:
                    pe.wait_ge(out_taken, u * 2 + qh + 1)
                for h in range(HQ):
                    last = nc.tensor.matmul(outb[32 * h:32 * h + 32, :], vu[:, b % 2, kt, h, :], probs[:, j % RING, h, :],
                                            start=kt == 0, stop=kt == TT - 1)
                last.then_inc(pv_done, 1)

            for t in range(PROLOGUE):
                if t >= TURN_BANKS:
                    pe.wait_ge(turn_taken, t - TURN_BANKS + 1)
                if t < MAXES:
                    take_max(0, 0, t, (t + SHIFT) % TURN_BANKS)
                elif t == MAXES:
                    turn_max(0, (t + SHIFT) % TURN_BANKS)
                else:
                    take_max(0, 1, t - MAXES - 1, (t + SHIFT) % TURN_BANKS)

            pe.wait_ge(fixed, 16 * n_fixed)

            def unit(g, b, last):
                u = g * B + b
                t = 0

                def take_turn(turn):
                    bank = t % TURN_BANKS
                    pe.wait_ge(turn_taken, bank_free(g, b, last, t))
                    if turn[0] == "max":
                        take_max(g + (b + turn[1]) // B, (b + turn[1]) % B, turn[2], bank)
                    elif turn[0] == "rows":
                        turn_max(u + 1, bank)
                    else:
                        turn_out(u - turn[1], turn[2], bank)

                for j, turns in enumerate(unit_turns(b, last)[:STEPS]):
                    others = [turn for turn in turns if turn[0] != "max"]
                    maxima = [turn for turn in turns if turn[0] == "max"]
                    for what in ORDER:
                        if what in "0123":
                            score(u, g, b, j, int(what))
                        elif what == "p" and j > 0:
                            products(u, b, j - 1)
                        elif what == "p" and b > 0:
                            products(u - 1, b - 1, STEPS - 1)
                        elif what == "m" and maxima:
                            take_turn(maxima.pop(0))
                            t += 1
                        elif what == "x" and others:
                            take_turn(others[0])
                            t += 1
                if b == B - 1:
                    products(u, b, STEPS - 1)
                    take_turn(("out", 0, 1))

            with pe.Fori(0, QUADS - 1) as g:
                for b in range(B):
                    unit(g, b, False)
            for b in range(B):
                unit(QUADS - 1, b, True)

        @block.scalar
        def _(act):
            act.sem_inc(exp_done, 2)
            act.sem_inc(out_taken, 1)

            def take_out(g, b, last, qh):
                u = g * B + b
                act.wait_ge(pv_done, u * STEPS + TT * (qh + 1) + RING)
                if qh == 1:
                    act.wait_ge(turn_ready, base(g, b, last) + place_of(("out", 0, 0), b, last) + 1)
                elif b > 0:
                    act.wait_ge(turn_ready, base(g, b, last) + place_of(("out", 1, 1), b, last) + 1)
                else:
                    act.wait_ge(turn_ready, base(g, b, last))
                dst = osb[:, ::-1] if first else osb[:, :]
                act.activation(dst, outb[:, :], ACT.Copy).then_inc(out_taken, 1)

            def unit(g, b, last):
                u = g * B + b
                for j in range(STEPS):
                    act.wait_ge(pv_done, u * STEPS + j + 1)
                    for hp in range(2):
                        act.wait_ge(score_ready, u * 2 * STEPS + 2 * j + hp + 1)
                        if hp == 1 and j in NEAR_STEPS:
                            act.wait_ge(added, u * len(NEAR_STEPS) + NEAR_STEPS.index(j) + 1)
                        act.activation(probs[:, j % RING, 2 * hp:2 * hp + 2, :], scores[:, hp, :, :], ACT.Exp).then_inc(exp_done, 1)
                    if j == 0 and b > 0:
                        take_out(g, b - 1, last, 1)
                    if j == TT:
                        take_out(g, b, last, 0)
                if b == B - 1:
                    take_out(g, b, last, 1)

            with act.Fori(0, QUADS - 1) as g:
                for b in range(B):
                    unit(g, b, False)
            for b in range(B):
                unit(QUADS - 1, b, True)

        @block.vector
        def _(dve):
            dve.sem_inc(pv_done, RING)

            def take_max(u, g, i, bank):
                h, t, hf = split_max(i)
                if first:
                    dve.sem_inc(gate, 1)
                    at = t * P + hf * HALF
                    dve.tensor_tensor_reduce(out=summed[:, i % 4, :], in0=turnb[:, bank, :], in1=strip[:, h, at:at + HALF],
                                             scale=1.0, scalar=-3e38, op0=ALU.add, op1=ALU.max,
                                             accum_out=mh[:, h, t, hf:hf + 1]).then_inc(turn_taken, 1)
                else:
                    dve.reduce_max(mh[:, h, t, hf:hf + 1], turnb[:, bank, :], axis=AX).then_inc(turn_taken, 1)

            def before_max(u, g, i):
                if i == 0 and not (isinstance(u, int) and u == 0):
                    dve.wait_ge(mq_done, u)
                if first and i % (2 * TT) == 0:
                    dve.wait_ge(strip_in[i // (2 * TT)], (g + 1) * 16)

            def join_max(taken):
                dve.wait_ge(turn_taken, taken)
                dve.reduce_max(mq[:, :, :].rearrange("p h t -> p (h t)"),
                               mh[:, :, :, :].rearrange("p h t a -> p (h t) a"), axis=AX).then_inc(mq_done, 1)

            def split_parts(u, bank, taken):
                dve.tensor_scalar(m1[:, :], turnb[0:HQ * TT, bank, 0:P], -1.0, None, ALU.mult).then_inc(turn_taken, 1)
                dve.wait_ge(turn_taken, taken)
                if not (isinstance(u, int) and u == 0):
                    dve.wait_ge(m_rows, u * 48)
                dve.tensor_copy(mparts[:, 0, :], m1[:, :]).then_inc(mstep, 1)
                dve.wait_ge(mstep, u * 3 + 1)
                dve.tensor_tensor(m2[:, :], m1[:, :], mparts[:, 0, :], ALU.subtract).then_inc(mstep, 1)
                dve.wait_ge(mstep, u * 3 + 2)
                dve.tensor_copy(mparts[:, 1, :], m2[:, :]).then_inc(mstep, 1)
                dve.wait_ge(mstep, u * 3 + 3)
                dve.tensor_tensor(mparts[:, 2, :], m2[:, :], mparts[:, 1, :], ALU.subtract).then_inc(mparts_done, 1)

            def normalise(u, g, b, qh, bank, turns_before):
                dve.wait_ge(turn_taken, turns_before)
                out = turnb[:, bank, :].rearrange("p (t h n) -> p t h n", t=4, n=32)
                dve.reciprocal(rz[:, :, :], out[:, :, :, DK]).then_inc(rz_done, 1)
                dve.wait_ge(rz_done, u * 2 + qh + 1)
                tile = b * TT + 4 * ((1 - qh) if first else qh)
                dve.tensor_tensor(v_sb[:, tile:tile + 4, bass.ds(g * HQ, HQ), :], out[:, :, :, 0:DK],
                                  rz[:, :, :].unsqueeze(3).to_broadcast([P, 4, HQ, DK]), ALU.mult).then_inc(turn_taken, 1)

            def add_bias(u, g, b, j):
                col, width, at = near_columns(j // TT, j % TT)
                if b == 0 and j == NEAR_STEPS[0]:
                    dve.wait_ge(near_in, (g + 1) * HQ * 16)
                dve.wait_ge(score_ready, u * 2 * STEPS + 2 * j + 2)
                part = scores[:, 1, :, col:col + width]
                dve.tensor_tensor(part, part, near_f[:, :, at:at + width], ALU.add).then_inc(added, 1)

            for t in range(PROLOGUE):
                if t < MAXES:
                    before_max(0, 0, t)
                    dve.wait_ge(turn_ready, t + 1)
                    take_max(0, 0, t, (t + SHIFT) % TURN_BANKS)
                elif t == MAXES:
                    join_max(t)
                    dve.wait_ge(turn_ready, t + 1)
                    split_parts(0, (t + SHIFT) % TURN_BANKS, t + 1)
                else:
                    before_max(1, 0, t - MAXES - 1)
                    dve.wait_ge(turn_ready, t + 1)
                    take_max(1, 0, t - MAXES - 1, (t + SHIFT) % TURN_BANKS)

            def unit(g, b, last):
                u = g * B + b
                t = base(g, b, last)
                local = 0
                for j, turns in enumerate(unit_turns(b, last)):
                    for n, turn in enumerate(turns):
                        bank = local % TURN_BANKS
                        ahead_g = g + (b + turn[1]) // B if turn[0] == "max" else g
                        if turn[0] == "max":
                            before_max(u + turn[1], ahead_g, turn[2])
                        dve.wait_ge(turn_ready, t + local + 1)
                        if turn[0] == "max":
                            take_max(u + turn[1], ahead_g, turn[2], bank)
                        elif turn[0] == "rows":
                            split_parts(u + 1, bank, t + local + 1)
                        else:
                            normalise(u - turn[1], g, b - turn[1], turn[2], bank, t + local)
                        local += 1
                        if turn == ("max", 1, MAXES - 1):
                            join_max(t + local)
                        if n == ADD_AFTER and j in NEAR_STEPS:
                            add_bias(u, g, b, j)
                    if len(turns) <= ADD_AFTER and j in NEAR_STEPS:
                        add_bias(u, g, b, j)

            with dve.Fori(0, QUADS - 1) as g:
                for b in range(B):
                    unit(g, b, False)
            for b in range(B):
                unit(QUADS - 1, b, True)


def negative_registers(nc, ident, v_sb, parts_dram, mask_dram, reg_sb):
    RQ = 32
    rows = ROWS_2["max"]
    n_loads = 2 * len(RUNS) + 1
    with ExitStack() as ctx:
        k = Kit(nc, ctx, "r2")
        q_sb = k.sb("q", [P, B, HQ, RQ], BF16)
        k_sb = k.sb("k", [P, B, HQ, S], BF16)
        bars = k.sb("bars", [1, 2, HQ, RQ], BF16)
        vu = k.sb("vu", [P, B, TT, HQ, DK + 1], F32)
        probs = k.sb("probs", [P, 2, S], F32)
        pT = k.sb("pT", [P, 2, TT, P], F32)
        nm = k.sb("nm", [P, 2], F32)
        rz = k.sb("rz", [RQ, HQ], F32)
        scores = k.ps("scores", [P, 2, S])
        turned = k.ps("turned", [P, TT, P])
        outb = k.ps("outb", [RQ, HALF])
        loaded = [k.sem(f"loaded{i}") for i in range(B)]
        fixed, bar_set, v_ready, score_ready, nm_done, exp_done, rz_done, turn_done, pT_done, pv_done, out_done = (
            k.sem(n) for n in ("fixed", "bar_set", "v_ready", "score_ready", "nm_done", "exp_done", "rz_done",
                               "turn_done", "pT_done", "pv_done", "out_done"))
        block = ctx.enter_context(nc.Block())

        @block.sync
        def _(sp):
            sp.wait_ge(bar_set, 2)
            for b in range(B):
                sp.dma_start(q_sb[TERM_ROWS:TERM_ROWS + 1, b, :, :], bars[:, 0]).then_inc(fixed, 16)
                sp.dma_start(q_sb[TERM_ROWS + 1:TERM_ROWS + 2, b, :, :], bars[:, 1]).then_inc(fixed, 16)

            def load(g, b):
                load_terms(sp, 0, parts_dram, q_sb[:, b], g, b, RQ, loaded[b])
                load_terms(sp, 1, parts_dram, k_sb[:, b], g, b, S, loaded[b])
                keys = mask_dram[2:4, b * S:(b + 1) * S].unsqueeze(1).to_broadcast([2, HQ, S])
                sp.dma_start(k_sb[TERM_ROWS:TERM_ROWS + 2, b, :, :], keys).then_inc(loaded[b], 16)

            for b in range(B):
                load(0, b)
            with sp.Fori(1, QUADS) as g:
                for b in range(B):
                    sp.wait_ge(score_ready, g * B + b - B + 1)
                    load(g, b)
            sp.wait_ge(fixed, 2 * B * 16)

        @block.gpsimd
        def _(pool):
            pool.memset(bars[:, 0], -BIG).then_inc(bar_set, 1)
            pool.memset(bars[:, 1], 0.0).then_inc(bar_set, 1)
            pool.memset(vu[:, :, :, :, DK:DK + 1], 1.0).then_inc(v_ready, 1)
            with pool.Fori(0, QUADS) as g:
                for b in range(B):
                    pool.wait_ge(pv_done, g * B + b + 1)
                    pool.tensor_copy(vu[:, b, :, :, 0:DK], v_sb[:, b * TT:(b + 1) * TT, bass.ds(g * HQ, HQ), :]).then_inc(v_ready, 1)

        @block.tensor
        def _(pe):
            pe.wait_ge(fixed, 2 * B * 16)

            def score(u, g, b):
                pe.wait_ge(loaded[b], (g + 1) * 16 * n_loads)
                pe.wait_ge(exp_done, u + 1)
                for hf in range(2):
                    for h in range(HQ):
                        last = nc.tensor.matmul(scores[32 * h:32 * h + 32, b % 2, hf * HALF:(hf + 1) * HALF],
                                                q_sb[0:rows, b, h, :], k_sb[0:rows, b, h, hf * HALF:(hf + 1) * HALF],
                                                start=True, stop=True)
                last.then_inc(score_ready, 1)

            def turn(u, b):
                pe.wait_ge(exp_done, u + 1 + 2)
                pe.wait_ge(pT_done, u + 1)
                for t in range(TT):
                    last = nc.tensor.transpose(turned[:, t, :], probs[:, b % 2, t * P:(t + 1) * P], ident[:, :])
                last.then_inc(turn_done, 1)

            def products(u, b):
                pe.wait_ge(pT_done, u + 2)
                pe.wait_ge(v_ready, u + 2)
                pe.wait_ge(out_done, u + 1)
                for h in range(HQ):
                    for t in range(TT):
                        last = nc.tensor.matmul(outb[:, h * (DK + 1):(h + 1) * (DK + 1)], pT[:, b % 2, t, 32 * h:32 * h + 32],
                                                vu[:, b, t, h, :], start=t == 0, stop=t == TT - 1)
                last.then_inc(pv_done, 1)

            def unit(g, b, last):
                u = g * B + b
                if not (last and b + 2 >= B):
                    score(u + 2, g + (b + 2) // B, (b + 2) % B)
                if not (last and b + 1 >= B):
                    turn(u + 1, b + 1)
                products(u, b)

            score(0, 0, 0)
            score(1, 0, 1)
            turn(0, 0)
            with pe.Fori(0, QUADS - 1) as g:
                for b in range(B):
                    unit(g, b, False)
            for b in range(B):
                unit(QUADS - 1, b, True)

        @block.scalar
        def _(act):
            act.sem_inc(exp_done, 2)
            act.sem_inc(pT_done, 1)

            def exps(u, i):
                act.wait_ge(nm_done, u + 1)
                act.wait_ge(turn_done, u + 1)
                act.activation(probs[:, i, :], scores[:, i, :], ACT.Exp, bias=nm[:, i:i + 1]).then_inc(exp_done, 1)

            def copy(u, i):
                act.wait_ge(turn_done, u + 1 + 2)
                act.wait_ge(pv_done, u + B - 1)
                act.activation(pT[:, i, :, :], turned[:, :, :], ACT.Copy).then_inc(pT_done, 1)

            def unit(g, b, last):
                u = g * B + b
                if not (last and b + 2 >= B):
                    exps(u + 2, b % 2)
                if not (last and b + 1 >= B):
                    copy(u + 1, (b + 1) % 2)

            exps(0, 0)
            exps(1, 1)
            copy(0, 0)
            with act.Fori(0, QUADS - 1) as g:
                for b in range(B):
                    unit(g, b, False)
            for b in range(B):
                unit(QUADS - 1, b, True)

        @block.vector
        def _(dve):
            dve.sem_inc(out_done, 1)
            dve.sem_inc(turn_done, 2)
            dve.sem_inc(pv_done, B)

            def top(u, i):
                dve.wait_ge(score_ready, u + 1)
                dve.tensor_reduce(nm[:, i:i + 1], scores[:, i, :], AX, ALU.max, negate=True).then_inc(nm_done, 1)

            def out(u, g, b):
                dve.wait_ge(pv_done, u + 1 + B)
                heads = outb[:, 0:HQ * (DK + 1)].rearrange("p (h d) -> p h d", d=DK + 1)
                dve.reciprocal(rz[:, :], heads[:, :, DK]).then_inc(rz_done, 1)
                dve.wait_ge(rz_done, u + 1)
                dve.tensor_tensor(reg_sb[:, b, bass.ds(g * HQ, HQ), :], heads[:, :, 0:DK],
                                  rz[:, :].unsqueeze(2).to_broadcast([RQ, HQ, DK]), ALU.mult).then_inc(out_done, 1)

            def unit(g, b, last):
                u = g * B + b
                if not (last and b + 2 >= B):
                    top(u + 2, b % 2)
                out(u, g, b)

            top(0, 0)
            top(1, 1)
            with dve.Fori(0, QUADS - 1) as g:
                for b in range(B):
                    unit(g, b, False)
            for b in range(B):
                unit(QUADS - 1, b, True)


def project(nc, layer, ident, v_sb, reg_sb, x_in, w_out, b_out, x_out):
    with ExitStack() as ctx:
        k = Kit(nc, ctx, f"o{layer}")
        second = layer == 2
        PAIRS = TT // 2
        w = k.sb("w", [P, 2, D], F32)
        bias = k.sb("bias", [P, D], F32)
        x = k.sb("x", [P, TT, D], F32)
        xb = k.sb("xb", [P, 2, TT, D], F32)
        aT = k.sb("aT", [P, 2, 2, 2, P], F32)
        y = k.sb("y", [P, 2, TT, D], F32)
        turned = k.ps("turned", [P, 2, HALF])
        outs = k.ps("outs", [P, 2, HALF])
        w_in, x_here, xb_done, xb_used, turn_done, aT_done, out_ready, y_done, stored = (
            k.sem(n) for n in ("w_in", "x_here", "xb_done", "xb_used", "turn_done", "aT_done", "out_ready", "y_done", "stored"))
        if second:
            mixed = k.sem("mixed")
        block = ctx.enter_context(nc.Block())
        x_v = x_in.rearrange("(b t p) d -> b p t d", p=P, t=TT)
        o_v = x_out.rearrange("(b t p) d -> b p t d", p=P, t=TT)

        @block.sync
        def _(sp):
            sp.dma_start(x[:, :, :], x_v[0]).then_inc(x_here, 16)
            sp.dma_start(w[:, :, :], w_out.rearrange("(c p) n -> p c n", p=P)).then_inc(w_in, 16)
            sp.dma_start(bias[:, :], b_out.rearrange("(a n) -> a n", a=1).to_broadcast([P, D])).then_inc(w_in, 16)

            def store(b, half):
                sp.wait_ge(y_done, (b + 1) * PAIRS)
                sp.wait_ge(stored, b * 16 + 32)
                sp.dma_start(o_v[bass.ds(b, 1)].rearrange("a p t d -> (a p) t d"), y[:, half, :, :]).then_inc(stored, 16)

            def batch(b, half):
                sp.wait_ge(xb_done, b + 1)
                sp.dma_start(x[:, :, :], x_v[bass.ds(b + 1, 1)].rearrange("a p t d -> (a p) t d")).then_inc(x_here, 16)
                store(b, half)

            with sp.Fori(0, B // 2 - 1) as pair:
                for half in range(2):
                    batch(2 * pair + half, half)
            batch(B - 2, 0)
            store(B - 1, 1)
            sp.wait_ge(stored, B * 16 + 32)

        @block.gpsimd
        def _(pool):
            pool.wait_ge(w_in, 32)
            with pool.Fori(0, B // 2) as pair:
                for half in range(2):
                    pool.wait_ge(x_here, (2 * pair + half + 1) * 16)
                    pool.wait_ge(xb_used, 2 * pair + half + 1)
                    pool.tensor_tensor(xb[:, half, :, :], x[:, :, :], bias[:, :].unsqueeze(1).to_broadcast([P, TT, D]),
                                       ALU.add).then_inc(xb_done, 1)

        @block.tensor
        def _(pe):
            pe.wait_ge(w_in, 32)
            if second:
                pe.wait_ge(mixed, 2)

            def turn(n, tile, i):
                pe.wait_ge(aT_done, n + 1)
                for a in range(2):
                    for c in range(2):
                        src = v_sb[:, tile + a, c * (H // 2):(c + 1) * (H // 2), :].rearrange("p h d -> p (h d)")
                        last = nc.tensor.transpose(turned[:, i, (2 * c + a) * P:(2 * c + a + 1) * P], src, ident[:, :])
                last.then_inc(turn_done, 1)

            def multiply(n, i):
                pe.wait_ge(aT_done, n + 1 + 2)
                for a in range(2):
                    for c in range(2):
                        last = nc.tensor.matmul(outs[:, i, a * D:(a + 1) * D], aT[:, i, c, a, :], w[:, c, :], start=c == 0, stop=c == 1)
                last.then_inc(out_ready, 1)

            turn(0, 0, 0)
            for n in range(B * PAIRS):
                if n + 1 < B * PAIRS:
                    turn(n + 1, 2 * (n + 1), (n + 1) % 2)
                if n >= 2:
                    pe.wait_ge(y_done, n - 1)
                multiply(n, n % 2)

        @block.scalar
        def _(act):
            act.sem_inc(aT_done, 2)
            act.sem_inc(out_ready, 1)
            with act.Fori(0, B) as b:
                for i in range(PAIRS):
                    act.wait_ge(turn_done, b * PAIRS + i + 1)
                    act.wait_ge(out_ready, b * PAIRS + max(i, 1))
                    act.activation(aT[:, i % 2].rearrange("p c a n -> p (c a n)"), turned[:, i % 2, :], ACT.Copy).then_inc(aT_done, 1)

        @block.vector
        def _(dve):
            if second:
                regs = v_sb[0:REG, 0:NT:TT, :, :]
                dve.tensor_tensor(regs, regs, reg_sb[0:REG, :, :, :], ALU.add).then_inc(mixed, 1)
                dve.wait_ge(mixed, 1)
                dve.tensor_scalar(regs, regs, 0.5, None, ALU.mult).then_inc(mixed, 1)
            dve.sem_inc(xb_used, 2)
            dve.sem_inc(stored, 32)
            with dve.Fori(0, B // 2) as pair:
                for half in range(2):
                    b = 2 * pair + half
                    dve.wait_ge(xb_done, b + 1)
                    dve.wait_ge(stored, b * 16 + 16)
                    for i in range(PAIRS):
                        dve.wait_ge(out_ready, b * PAIRS + i + 1 + 1)
                        dve.tensor_tensor(y[:, half, 2 * i:2 * i + 2, :], outs[:, i % 2, :].rearrange("p (a d) -> p a d", d=D),
                                          xb[:, half, 2 * i:2 * i + 2, :], ALU.add).then_inc(y_done, 1)
                    dve.wait_ge(y_done, (b + 1) * PAIRS)
                    dve.sem_inc(xb_used, 1)


def two_layers(nc, x, w_qkv1, b_qkv1, w_out1, b_out1, rel_bias, g_info, w_qkv2, w_proj2, b_proj2, out):
    scratch = lambda name, shape, dt: nc.dram_tensor(name, shape, dt, kind="Internal").ap()
    parts1 = scratch("parts1", (2, H, 3, DK, B * S), BF16)
    parts2 = scratch("parts2", (2, H, 3, DK, B * S), BF16)
    line = scratch("line", (H, EXT), F32)
    near = scratch("near", (H, 3, NEAR_W + P), BF16)
    far = scratch("far", (H, FAR_ROWS, S), BF16)
    mask = scratch("mask", (4, B * S), BF16)
    x1 = scratch("x1", (B * S, D), F32)
    x_rows = x.rearrange("b s d -> (b s) d")
    out_rows = out.rearrange("b s d -> (b s) d")
    with ExitStack() as ctx:
        keep = Kit(nc, ctx, "k")
        ident, identb = constants(nc, keep)
        v_sb = keep.sb("v", [P, NT, H, DK], F32)
        bias_lines(nc, ident, rel_bias, line, near, far)
        prepare(nc, 1, ident, x_rows, w_qkv1, b_qkv1, None, v_sb, parts1, None)
        attend(nc, 1, ident, identb, v_sb, parts1, None, line, near, far)
        project(nc, 1, ident, v_sb, None, x_rows, w_out1, b_out1, x1)
        prepare(nc, 2, ident, x1, w_qkv2, None, g_info, v_sb, parts2, mask)
        reg_sb = keep.sb("reg", [32, B, H, DK], F32)
        negative_registers(nc, ident, v_sb, parts2, mask, reg_sb)
        attend(nc, 2, ident, identb, v_sb, parts2, mask, None, None, None)
        project(nc, 2, ident, v_sb, reg_sb, x1, w_proj2, b_proj2, out_rows)


_INS = ['L0_attn_x', 'L0_attn_W_qkv', 'L0_attn_b_qkv', 'L0_attn_W_out', 'L0_attn_b_out', 'L0_attn_rel_bias',
        'L0_ffn_g_info', 'L0_ffn_W_qkv', 'L0_ffn_W_proj', 'L0_ffn_b_proj']


def kernel(**inputs):
    import numpy as _np
    import concourse.bacc as _bacc
    from concourse.bass_utils import run_bass_kernel_spmd as _run

    nc = _bacc.Bacc("TRN2", target_bir_lowering=False, num_devices=1)
    arrays, args = {}, []
    for name in _INS:
        a = _np.ascontiguousarray(inputs[name])
        arrays[f"in_{name}"] = a
        args.append(nc.dram_tensor(f"in_{name}", a.shape, mybir.dt.from_np(a.dtype), kind="ExternalInput").ap())
    out = nc.dram_tensor("out", (B, S, D), F32, kind="ExternalOutput").ap()
    two_layers(nc, *args, out)
    r = _run(nc, [arrays], core_ids=[0])
    return r.results[0]["out"]
```
